# Optimizing a Trainium2 kernel written in Bass

```python
import numpy as np
import jax
import jax.numpy as jnp

def _softmax(x, axis=-1):
    return jax.nn.softmax(x, axis=axis)

def _gelu(x):
    return jax.nn.gelu(x, approximate=True)

def _silu(x):
    return jax.nn.silu(x)

def _sigmoid(x):
    return jax.nn.sigmoid(x)

def _layernorm(x, axis=-1, eps=1e-05):
    m = jnp.mean(x, axis=axis, keepdims=True)
    v = jnp.var(x, axis=axis, keepdims=True)
    return (x - m) / jnp.sqrt(v + eps)

def _scatter_add(tgt, idx, src, axis=0):
    return tgt.at[idx].add(src)

def _segment_sum(src, seg, n):
    return jax.ops.segment_sum(src, seg, n)
kernel_name = 'mk_gps_d1_gnn_r8_2b0b88'

def setup_inputs(seed: int=0):
    np.random.seed(seed)
    _w = jnp.asarray

    def _rec_inputs():
        import jax
        import jax.numpy as jnp
        _gk = jax.random.key(seed)
        x = -0.0002117 + 1 * jax.random.normal(jax.random.fold_in(_gk, 1), (12500, 256), jnp.float32)
        _s = jax.random.randint(jax.random.fold_in(_gk, 2), (100000,), 0, 12500, jnp.int32)
        _d = jax.random.randint(jax.random.fold_in(_gk, 3), (100000,), 0, 12500, jnp.int32)
        _loop = jnp.arange(12500, dtype=jnp.int32)
        src = jnp.concatenate([_s, _d, _loop])
        dst = jnp.concatenate([_d, _s, _loop])
        _o = jnp.argsort(dst, stable=True)
        src = src[_o]
        dst = dst[_o]
        return (x, src, dst)
    x, src, dst = _rec_inputs()

    def _L0_gnn_setup():
        import jax, jax.numpy as jnp
        import numpy as np
        N = 12500
        E = 100000
        IN = 256
        H = 8
        D = 32
        HD = H * D
        HID = 128
        NEG_SLOPE = 0.2

        def _gat(h, W_fc, attn_l, attn_r, bias, src, dst):
            feat = (h @ W_fc).reshape(N, H, D)
            el = jnp.sum(feat * attn_l, axis=-1)
            er = jnp.sum(feat * attn_r, axis=-1)
            e = jax.nn.leaky_relu(el[src] + er[dst], NEG_SLOPE)
            mx = jax.ops.segment_max(e, dst, num_segments=N)
            mx = jnp.where(jnp.isfinite(mx), mx, 0.0)
            ee = jnp.exp(e - mx[dst])
            denom = jax.ops.segment_sum(ee, dst, num_segments=N)
            alpha = ee / denom[dst]
            msg = feat[src] * alpha[:, :, None]
            rst = jax.ops.segment_sum(msg, dst, num_segments=N)
            rst = rst + bias.reshape(H, D)
            return jax.nn.elu(rst).reshape(N, HD)
        key = jax.random.key(seed)
        ks = jax.random.split(key, 10)
        h = jax.random.normal(ks[0], (N, IN), dtype=jnp.float32)
        src = jax.random.randint(ks[1], (E,), 0, N)
        dst = jax.random.randint(ks[2], (E,), 0, N)
        s = 0.05
        W_fc = jax.random.normal(ks[3], (IN, HD), dtype=jnp.float32) * s
        attn_l = jax.random.normal(ks[4], (H, D), dtype=jnp.float32) * s
        attn_r = jax.random.normal(ks[5], (H, D), dtype=jnp.float32) * s
        bias = jnp.zeros((HD,), dtype=jnp.float32)
        sem_W1 = jax.random.normal(ks[6], (HD, HID), dtype=jnp.float32) * s
        sem_b1 = jnp.zeros((HID,), dtype=jnp.float32)
        sem_W2 = jax.random.normal(ks[7], (HID, 1), dtype=jnp.float32) * s
        return {'h': h, 'W_fc': W_fc, 'attn_l': attn_l, 'attn_r': attn_r, 'bias': bias, 'sem_W1': sem_W1, 'sem_b1': sem_b1, 'sem_W2': sem_W2, 'src': src, 'dst': dst}
    _L0_gnn_all = _L0_gnn_setup()
    _L0_gnn_in = {k: v for k, v in _L0_gnn_all.items() if k in ('W_fc', 'attn_l', 'attn_r', 'bias', 'sem_W1', 'sem_b1', 'sem_W2')}
    del _L0_gnn_all

    def _L0_mix_setup():
        import jax, jax.numpy as jnp
        import numpy as np
        D_MODEL = 256
        NHEAD = 8
        D_HEAD = D_MODEL // NHEAD
        DIM_FF = 1024
        B, L = (4, 2048)
        LN_EPS = 1e-05

        def _layernorm(x, g, b):
            mu = jnp.mean(x, axis=-1, keepdims=True)
            var = jnp.mean((x - mu) ** 2, axis=-1, keepdims=True)
            return (x - mu) * jax.lax.rsqrt(var + LN_EPS) * g + b

        def _phi(x):
            return jnp.where(x > 0, x + 1.0, jnp.exp(x))
        key = jax.random.key(seed)
        ks = jax.random.split(key, 16)
        s_in = 1.0 / np.sqrt(D_MODEL)
        s_ff = 1.0 / np.sqrt(DIM_FF)
        inp = {'x': jax.random.normal(ks[0], (B, L, D_MODEL), dtype=jnp.float32), 'Wq': jax.random.normal(ks[1], (D_MODEL, D_MODEL), dtype=jnp.float32) * s_in, 'bq': jnp.zeros((D_MODEL,), jnp.float32), 'Wk': jax.random.normal(ks[2], (D_MODEL, D_MODEL), dtype=jnp.float32) * s_in, 'bk': jnp.zeros((D_MODEL,), jnp.float32), 'Wv': jax.random.normal(ks[3], (D_MODEL, D_MODEL), dtype=jnp.float32) * s_in, 'bv': jnp.zeros((D_MODEL,), jnp.float32), 'Wo': jax.random.normal(ks[4], (D_MODEL, D_MODEL), dtype=jnp.float32) * s_in, 'bo': jnp.zeros((D_MODEL,), jnp.float32), 'W1': jax.random.normal(ks[5], (D_MODEL, DIM_FF), dtype=jnp.float32) * s_in, 'b1': jnp.zeros((DIM_FF,), jnp.float32), 'W2': jax.random.normal(ks[6], (DIM_FF, D_MODEL), dtype=jnp.float32) * s_ff, 'b2': jnp.zeros((D_MODEL,), jnp.float32), 'ln1_g': jnp.ones((D_MODEL,), jnp.float32), 'ln1_b': jnp.zeros((D_MODEL,), jnp.float32), 'ln2_g': jnp.ones((D_MODEL,), jnp.float32), 'ln2_b': jnp.zeros((D_MODEL,), jnp.float32)}
        return inp
    _L0_mix_all = _L0_mix_setup()
    _L0_mix_in = {k: v for k, v in _L0_mix_all.items() if k in ('Wq', 'bq', 'Wk', 'bk', 'Wv', 'bv', 'Wo', 'bo', 'W1', 'b1', 'W2', 'b2', 'ln1_g', 'ln1_b', 'ln2_g', 'ln2_b')}
    del _L0_mix_all

    def _L0_ffn_setup():
        import jax, jax.numpy as jnp
        import numpy as np
        E, D, H, TOP_K = (6, 256, 256, 2)
        ROUTER_H = D // 2
        key = jax.random.key(seed)
        ks = jax.random.split(key, 12)
        s = 1.0 / np.sqrt(D)
        sh = 1.0 / np.sqrt(H)
        sr = 1.0 / np.sqrt(ROUTER_H)
        return {'features': jax.random.normal(ks[0], (8, 512, D), dtype=jnp.float32), 'router_w1': jax.random.uniform(ks[1], (D, ROUTER_H), jnp.float32, -s, s), 'router_b1': jnp.zeros((ROUTER_H,), jnp.float32), 'router_w2': jax.random.uniform(ks[2], (ROUTER_H, E), jnp.float32, -sr, sr), 'router_b2': jnp.zeros((E,), jnp.float32), 'expert_w1': jax.random.uniform(ks[3], (E, D, H), jnp.float32, -s, s), 'expert_b1': jnp.zeros((E, H), jnp.float32), 'expert_w2': jax.random.uniform(ks[4], (E, H, H), jnp.float32, -sh, sh), 'expert_b2': jnp.zeros((E, H), jnp.float32), 'expert_w3': jax.random.uniform(ks[5], (E, H, D), jnp.float32, -sh, sh), 'expert_b3': jnp.zeros((E, D), jnp.float32)}
    _L0_ffn_all = _L0_ffn_setup()
    _L0_ffn_in = {k: v for k, v in _L0_ffn_all.items() if k in ('router_w1', 'router_b1', 'router_w2', 'router_b2', 'expert_w1', 'expert_b1', 'expert_w2', 'expert_b2', 'expert_w3', 'expert_b3')}
    del _L0_ffn_all
    return {'x': x, 'src': src, 'dst': dst, 'L0_gnn_W_fc': _L0_gnn_in['W_fc'], 'L0_gnn_attn_l': _L0_gnn_in['attn_l'], 'L0_gnn_attn_r': _L0_gnn_in['attn_r'], 'L0_gnn_bias': _L0_gnn_in['bias'], 'L0_gnn_sem_W1': _L0_gnn_in['sem_W1'], 'L0_gnn_sem_b1': _L0_gnn_in['sem_b1'], 'L0_gnn_sem_W2': _L0_gnn_in['sem_W2'], 'L0_mix_Wq': _L0_mix_in['Wq'], 'L0_mix_bq': _L0_mix_in['bq'], 'L0_mix_Wk': _L0_mix_in['Wk'], 'L0_mix_bk': _L0_mix_in['bk'], 'L0_mix_Wv': _L0_mix_in['Wv'], 'L0_mix_bv': _L0_mix_in['bv'], 'L0_mix_Wo': _L0_mix_in['Wo'], 'L0_mix_bo': _L0_mix_in['bo'], 'L0_mix_W1': _L0_mix_in['W1'], 'L0_mix_b1': _L0_mix_in['b1'], 'L0_mix_W2': _L0_mix_in['W2'], 'L0_mix_b2': _L0_mix_in['b2'], 'L0_mix_ln1_g': _L0_mix_in['ln1_g'], 'L0_mix_ln1_b': _L0_mix_in['ln1_b'], 'L0_mix_ln2_g': _L0_mix_in['ln2_g'], 'L0_mix_ln2_b': _L0_mix_in['ln2_b'], 'L0_ffn_router_w1': _L0_ffn_in['router_w1'], 'L0_ffn_router_b1': _L0_ffn_in['router_b1'], 'L0_ffn_router_w2': _L0_ffn_in['router_w2'], 'L0_ffn_router_b2': _L0_ffn_in['router_b2'], 'L0_ffn_expert_w1': _L0_ffn_in['expert_w1'], 'L0_ffn_expert_b1': _L0_ffn_in['expert_b1'], 'L0_ffn_expert_w2': _L0_ffn_in['expert_w2'], 'L0_ffn_expert_b2': _L0_ffn_in['expert_b2'], 'L0_ffn_expert_w3': _L0_ffn_in['expert_w3'], 'L0_ffn_expert_b3': _L0_ffn_in['expert_b3']}

def reference(x, src, dst, L0_gnn_W_fc, L0_gnn_attn_l, L0_gnn_attn_r, L0_gnn_bias, L0_gnn_sem_W1, L0_gnn_sem_b1, L0_gnn_sem_W2, L0_mix_Wq, L0_mix_bq, L0_mix_Wk, L0_mix_bk, L0_mix_Wv, L0_mix_bv, L0_mix_Wo, L0_mix_bo, L0_mix_W1, L0_mix_b1, L0_mix_W2, L0_mix_b2, L0_mix_ln1_g, L0_mix_ln1_b, L0_mix_ln2_g, L0_mix_ln2_b, L0_ffn_router_w1, L0_ffn_router_b1, L0_ffn_router_w2, L0_ffn_router_b2, L0_ffn_expert_w1, L0_ffn_expert_b1, L0_ffn_expert_w2, L0_ffn_expert_b2, L0_ffn_expert_w3, L0_ffn_expert_b3):
    import jax
    import jax.numpy as jnp

    def _L0_gnn_ref(h, W_fc, attn_l, attn_r, bias, sem_W1, sem_b1, sem_W2, src, dst):
        import jax, jax.numpy as jnp
        import numpy as np
        N = 12500
        E = 100000
        IN = 256
        H = 8
        D = 32
        HD = H * D
        HID = 128
        NEG_SLOPE = 0.2

        def _gat(h, W_fc, attn_l, attn_r, bias, src, dst):
            feat = (h @ W_fc).reshape(N, H, D)
            el = jnp.sum(feat * attn_l, axis=-1)
            er = jnp.sum(feat * attn_r, axis=-1)
            e = jax.nn.leaky_relu(el[src] + er[dst], NEG_SLOPE)
            mx = jax.ops.segment_max(e, dst, num_segments=N)
            mx = jnp.where(jnp.isfinite(mx), mx, 0.0)
            ee = jnp.exp(e - mx[dst])
            denom = jax.ops.segment_sum(ee, dst, num_segments=N)
            alpha = ee / denom[dst]
            msg = feat[src] * alpha[:, :, None]
            rst = jax.ops.segment_sum(msg, dst, num_segments=N)
            rst = rst + bias.reshape(H, D)
            return jax.nn.elu(rst).reshape(N, HD)
        out = _gat(h, W_fc, attn_l, attn_r, bias, src, dst)
        z = out[:, None, :]
        w = (jnp.tanh(z @ sem_W1 + sem_b1) @ sem_W2).mean(0)
        beta = jax.nn.softmax(w, axis=0)
        return jnp.sum(beta * z, axis=1)

    def _L0_mix_ref(x, Wq, bq, Wk, bk, Wv, bv, Wo, bo, W1, b1, W2, b2, ln1_g, ln1_b, ln2_g, ln2_b):
        import jax, jax.numpy as jnp
        import numpy as np
        D_MODEL = 256
        NHEAD = 8
        D_HEAD = D_MODEL // NHEAD
        DIM_FF = 1024
        B, L = (4, 2048)
        LN_EPS = 1e-05

        def _layernorm(x, g, b):
            mu = jnp.mean(x, axis=-1, keepdims=True)
            var = jnp.mean((x - mu) ** 2, axis=-1, keepdims=True)
            return (x - mu) * jax.lax.rsqrt(var + LN_EPS) * g + b

        def _phi(x):
            return jnp.where(x > 0, x + 1.0, jnp.exp(x))
        Bq, Lq, _ = x.shape
        q = (x @ Wq + bq).reshape(Bq, Lq, NHEAD, D_HEAD)
        k = (x @ Wk + bk).reshape(Bq, Lq, NHEAD, D_HEAD)
        v = (x @ Wv + bv).reshape(Bq, Lq, NHEAD, D_HEAD)
        q_phi = _phi(q)
        k_phi = _phi(k)
        kv = jnp.einsum('blhd,blhe->bhde', k_phi, v)
        k_sum = k_phi.sum(axis=1)
        z = 1.0 / (jnp.einsum('blhd,bhd->blh', q_phi, k_sum) + 1e-06)
        out = jnp.einsum('blhd,bhde,blh->blhe', q_phi, kv, z)
        out = out.reshape(Bq, Lq, D_MODEL) @ Wo + bo
        x = _layernorm(x + out, ln1_g, ln1_b)
        ff = jax.nn.relu(x @ W1 + b1) @ W2 + b2
        x = _layernorm(x + ff, ln2_g, ln2_b)
        return x

    def _L0_ffn_ref(features, router_w1, router_b1, router_w2, router_b2, expert_w1, expert_b1, expert_w2, expert_b2, expert_w3, expert_b3):
        import jax, jax.numpy as jnp
        import numpy as np
        E, D, H, TOP_K = (6, 256, 256, 2)
        ROUTER_H = D // 2
        rh = jax.nn.relu(features @ router_w1 + router_b1)
        expert_logits = jax.nn.softmax(rh @ router_w2 + router_b2, axis=-1)
        top_w, top_i = jax.lax.top_k(expert_logits, TOP_K)
        routing_weights = jax.nn.softmax(top_w, axis=-1)
        h1 = jax.nn.relu(jnp.einsum('bsd,edh->bseh', features, expert_w1) + expert_b1)
        h2 = jax.nn.relu(jnp.einsum('bseh,ehf->bsef', h1, expert_w2) + expert_b2)
        expert_out = jnp.einsum('bsef,efo->bseo', h2, expert_w3) + expert_b3
        sel = jnp.take_along_axis(expert_out, top_i[:, :, :, None], axis=2)
        combined = jnp.sum(sel * routing_weights[..., None], axis=2)
        return combined
    xn = _layernorm(x, axis=-1)
    x = x + _L0_gnn_ref(xn, L0_gnn_W_fc, L0_gnn_attn_l, L0_gnn_attn_r, L0_gnn_bias, L0_gnn_sem_W1, L0_gnn_sem_b1, L0_gnn_sem_W2, src, dst) + _L0_mix_ref(xn[None], L0_mix_Wq, L0_mix_bq, L0_mix_Wk, L0_mix_bk, L0_mix_Wv, L0_mix_bv, L0_mix_Wo, L0_mix_bo, L0_mix_W1, L0_mix_b1, L0_mix_W2, L0_mix_b2, L0_mix_ln1_g, L0_mix_ln1_b, L0_mix_ln2_g, L0_mix_ln2_b)[0]
    x = x + _L0_ffn_ref(_layernorm(x, axis=-1)[None], L0_ffn_router_w1, L0_ffn_router_b1, L0_ffn_router_w2, L0_ffn_router_b2, L0_ffn_expert_w1, L0_ffn_expert_b1, L0_ffn_expert_w2, L0_ffn_expert_b2, L0_ffn_expert_w3, L0_ffn_expert_b3)[0]
    return x

_drawn_inputs = setup_inputs


def setup_inputs(seed=0):
    import zlib

    import numpy as np

    out = dict(_drawn_inputs(seed))
    spreads = {'L0_gnn_bias': (0.0, 0.1),
     'L0_gnn_sem_b1': (0.0, 0.1),
     'L0_mix_bq': (0.0, 0.8),
     'L0_mix_bk': (0.0, 0.8),
     'L0_mix_bv': (0.0, 0.1),
     'L0_mix_bo': (0.0, 0.1),
     'L0_mix_b1': (0.0, 0.1),
     'L0_mix_b2': (0.0, 0.1),
     'L0_mix_ln1_g': (1.0, 0.2),
     'L0_mix_ln1_b': (0.0, 0.1),
     'L0_mix_ln2_g': (1.0, 0.2),
     'L0_mix_ln2_b': (0.0, 0.1),
     'L0_ffn_router_b1': (0.0, 0.394),
     'L0_ffn_router_b2': (0.0, 0.1),
     'L0_ffn_expert_b1': (0.0, 0.8),
     'L0_ffn_expert_b2': (0.0, 0.557),
     'L0_ffn_expert_b3': (0.0, 0.1)}
    factors = {'L0_gnn_attn_l': 2.978,
     'L0_gnn_attn_r': 7.808,
     'L0_mix_Wq': 8.0,
     'L0_mix_Wk': 8.0,
     'L0_mix_Wv': 7.381}
    for name, (base, spread) in spreads.items():
        noise = np.random.default_rng([zlib.crc32(name.encode()), seed]).standard_normal(out[name].shape)
        drawn = base * np.exp(spread * noise) if base else spread * noise
        out[name] = jnp.asarray(drawn.astype(out[name].dtype))
    for name, factor in factors.items():
        out[name] = (out[name] * factor).astype(out[name].dtype)
    return out
```

```python
import numpy as np
import concourse.bass as bass
from concourse import mybir
from contextlib import ExitStack

N, E, D, H, DH = 12500, 212500, 256, 8, 32
P = 125
BLOCKS, TILES = N // P, E // P
BATCH = 8
RING = 3
UNITS = 1800
BATCHES = UNITS // BATCH
UG, UP = 15, 120
ROW = D + H
FF, EXPERTS, RH = 1024, 6, 128
EPS, ATT_EPS, SLOPE = 1e-5, 1e-6, 0.2
TINY, LOW = 1e-37, -1e30
HALF = 128
C_RS = 13
CONSTS = ["c_ident", "c_headmask", "c_iota", "c_jcol", "c_tile", "c_unit", "c_attnmask"]


def shape_constants():
    f = np.float32
    c = {}
    c["c_ident"] = np.eye(128, dtype=f)
    c["c_headmask"] = np.kron(np.eye(4), np.ones((DH, DH))).astype(f)
    c["c_iota"] = np.tile(np.arange(P, dtype=f), (P, 1))
    c["c_jcol"] = np.arange(P, dtype=f)[:, None].copy()
    c["c_tile"] = np.arange(TILES, dtype=f).reshape(100, 17)
    c["c_unit"] = np.arange(UNITS, dtype=f).reshape(UG, UP).T.copy()
    m = np.zeros((2, HALF, H), f)
    for h in range(H):
        m[h // 4, DH * (h % 4):DH * (h % 4) + DH, h] = 1
    c["c_attnmask"] = np.ascontiguousarray(m.transpose(1, 0, 2))
    return c


def inverse_sqrt(nc, link, var, rs):
    ALU, i32 = mybir.AluOpType, mybir.dt.int32
    TS, STT = nc.vector.tensor_scalar, nc.vector.scalar_tensor_tensor
    ve, nh, t, y0, y = [rs[:, j] for j in range(5)]
    link(TS(ve, var, EPS, None, ALU.add))
    link(TS(nh, ve, -0.5, None, ALU.mult))
    link(TS(t.bitcast(i32), ve.bitcast(i32), 1, None, ALU.logical_shift_right))
    link(TS(y0.bitcast(i32), t.bitcast(i32), -1.0, float(0x5f3759df), ALU.mult, ALU.add))
    cur, other = y0, y
    for _ in range(3):
        link(STT(t, cur, 1.0, cur, ALU.mult, ALU.mult))
        link(nc.vector.tensor_tensor(t, t, nh, ALU.mult))
        link(STT(other, t, 1.5, cur, ALU.add, ALU.mult))
        cur, other = other, cur


def build(nc, a):
    f32, i32, u32 = mybir.dt.float32, mybir.dt.int32, mybir.dt.uint32
    ALU, ACT, AX = mybir.AluOpType, mybir.ActivationFunctionType, mybir.AxisListType
    ctx = ExitStack()
    with ctx:
        def sb(name, shape, dt=f32, where=None):
            return (where or ctx).enter_context(nc.sbuf_tensor(name, shape, dt))

        def pb(name, where=None):
            return (where or ctx).enter_context(nc.psum_tensor(name, [128, 512], f32))

        def sems(where, names):
            return {n: where.enter_context(nc.semaphore(n)) for n in names.split()}

        table = nc.dram_tensor("feat_table", (N, ROW), f32).ap()
        xn_dram = nc.dram_tensor("xn_dram", (N + 2 * P, D), f32).ap()
        key_dram = nc.dram_tensor("key_dram", (TILES,), f32).ap()
        blk_dram = nc.dram_tensor("blk_dram", (UNITS,), f32).ap()
        dl_dram = nc.dram_tensor("dl_dram", (UNITS + BATCH, P), f32).ap()

        ident = sb("ident", [128, 128])
        headmask = sb("headmask", [128, 128])
        iota = sb("iota", [P, P])
        jcol = sb("jcol", [P, 1])
        elr = sb("elr", [P, BLOCKS + 1, 2 * H])
        KV = sb("KV", [128, 2, HALF])
        KS = sb("KS", [128, 2, HALF])
        srcT = sb("srcT", [P, UNITS], i32)
        dlT = sb("dlT", [P, UNITS + BATCH])
        blk_tab = sb("blk_tab", [1, UNITS + BATCH], i32)
        last_tab = sb("last_tab", [1, UNITS], i32)
        mg_row = sb("mg_row", [P, H])
        ones = sb("ones", [128, 128])

        x_rows = a["x"]
        src_tiles = a["src"].rearrange("(t p) -> t p", p=P)
        dst_tiles = a["dst"].rearrange("(t p) -> t p", p=P)

        def halves(w):
            return w.rearrange("(k p) n -> p k n", p=HALF)

        def column(v, n):
            return v.rearrange("(k p) -> p k", p=n)

        def row(v, parts):
            return v.rearrange("(o n) -> o n", o=1).broadcast_to((parts, v.shape[0]))

        def tick_wait(eng, sem, value, tick):
            eng.wait_ge(sem, value)
            eng.sem_inc(tick, 1)

        with ExitStack() as st:
            wfc = sb("wfc", [128, 2, D], where=st)
            wfcT = sb("wfcT", [128, 2, D], where=st)
            amask = sb("amask", [128, 2, H], where=st)
            acol = sb("acol", [128, 2, 2], where=st)
            adiag = sb("adiag", [128, 2, 2 * H], where=st)
            wfe = sb("wfe", [128, 2, D + 2 * H], where=st)
            wkv = sb("wkv", [128, 2, 2 * D], where=st)
            bkv = sb("bkv", [P, 2 * D], where=st)
            xin = sb("xin", [P, 2, D], where=st)
            stat = sb("stat", [P, 2, 6], where=st)
            mv = sb("mv", [P, 2, 2], where=st)
            rstd = sb("rstd", [P, 5, 2], where=st)
            xn = sb("xn", [P, 2, D], where=st)
            xnT = sb("xnT", [128, 2, 2, P], where=st)
            fe = sb("fe", [P, 2, ROW], where=st)
            kpre = sb("kpre", [P, 2, D], where=st)
            kneg = sb("kneg", [P, 2, D], where=st)
            kexp = sb("kexp", [P, 2, D], where=st)
            kphi = sb("kphi", [P, 2, D], where=st)
            vv = sb("vv", [P, 2, 2, HALF + 1], where=st)
            zero = sb("zero", [128, 2 * (HALF + 1)], where=st)
            ps_t = [pb(f"ps_t{i}", st) for i in range(2)]
            ps_f = [pb(f"ps_f{i}", st) for i in range(2)]
            ps_kv = [pb(f"ps_kv{i}", st) for i in range(2)]
            ps_acc = pb("ps_acc", st)
            s = sems(st, "w_in c_in setup wt_ps wt_sb ad we_ps we_sb x_in0 x_in1 x_free stats mean rs xn_rdy "
                         "xn_st0 xn_st1 xt_ps xt_sb f_ps kv_ps f_sb el_sb k_pre fin_v fin_a fin_p v_sb k_neg k_exp k_phi kv_acc "
                         "f_st0 f_st1 fin pad_st mgp mgt mg1 mg8 mgd mgps pad_ld")
            x_in, xn_st, f_st = [s["x_in0"], s["x_in1"]], [s["xn_st0"], s["xn_st1"]], [s["f_st0"], s["f_st1"]]
            with nc.Block() as block:
                @block.sync
                def _(sp):
                    sp.dma_start(wfc[:], halves(a["L0_gnn_W_fc"])).then_inc(s["w_in"], 16)
                    sp.dma_start(wkv[:, :, 0:D], halves(a["L0_mix_Wk"])).then_inc(s["w_in"], 16)
                    sp.dma_start(wkv[:, :, D:2 * D], halves(a["L0_mix_Wv"])).then_inc(s["w_in"], 16)
                    sp.dma_start(bkv[:, 0:D], row(a["L0_mix_bk"], P)).then_inc(s["w_in"], 16)
                    sp.dma_start(bkv[:, D:2 * D], row(a["L0_mix_bv"], P)).then_inc(s["w_in"], 16)
                    with nc.allow_non_contiguous_dma(reason="256 scores' weights as a column"):
                        for j, name in enumerate(("L0_gnn_attn_l", "L0_gnn_attn_r")):
                            v = a[name].rearrange("(k h) d -> (h d) k", k=2)
                            for k in range(2):
                                sp.dma_start(acol[:, k, j:j + 1], v[:, k:k + 1]).then_inc(s["w_in"], 16)
                    sp.dma_start(ident[:], a["c_ident"]).then_inc(s["c_in"], 16)
                    sp.dma_start(headmask[:], a["c_headmask"]).then_inc(s["c_in"], 16)
                    sp.dma_start(iota[:], a["c_iota"]).then_inc(s["c_in"], 16)
                    sp.dma_start(jcol[:], a["c_jcol"]).then_inc(s["c_in"], 16)
                    sp.dma_start(amask[:], a["c_attnmask"]).then_inc(s["c_in"], 16)
                    with sp.Fori(0, BLOCKS // 2) as i:
                        for k in range(2):
                            t = i * 2 + k
                            sp.wait_ge(s["x_free"], t + 1)
                            sp.dma_start(xin[:, k, :], x_rows[bass.ds(t * P, P), :]).then_inc(x_in[k], 16)
                    sp.wait_ge(xn_st[1], 16 * (BLOCKS // 2))
                    sp.dma_start(xin[:, 0, :], xn_dram[0:P, :]).then_inc(s["pad_ld"], 16)
                    sp.wait_ge(s["pad_ld"], 16)
                    for j in range(2):
                        sp.dma_start(xn_dram[N + j * P:N + (j + 1) * P, :], xin[:, 0, :]).then_inc(s["pad_st"], 16)
                    sp.wait_ge(s["pad_st"], 32)
                    for k in range(2):
                        sp.wait_ge(xn_st[k], 16 * (BLOCKS // 2))
                        sp.wait_ge(f_st[k], 16 * (BLOCKS // 2))

                @block.gpsimd
                def _(pool):
                    nc.gpsimd.memset(zero[:], 0.0).then_inc(s["setup"], 1)
                    nc.gpsimd.memset(ones[:], 1.0).then_inc(s["setup"], 1)
                    nc.gpsimd.memset(elr[:, BLOCKS, :], 0.0).then_inc(s["setup"], 1)
                    for k in range(2):
                        nc.gpsimd.memset(vv[:, k, :, HALF:HALF + 1], 1.0).then_inc(s["setup"], 1)
                    with pool.Fori(0, BLOCKS // 2) as i:
                        for k in range(2):
                            t = i * 2 + k
                            tick_wait(pool, s["xn_rdy"], t + 1, s["fin"])
                            pool.dma_start(xn_dram[bass.ds(t * P, P), :], xn[:, k, :]).then_inc(xn_st[k], 16)
                        for k in range(2):
                            t = i * 2 + k
                            tick_wait(pool, s["el_sb"], t + 1, s["fin"])
                            pool.dma_start(table[bass.ds(t * P, P), :], fe[:, k, :]).then_inc(f_st[k], 16)

                @block.vector
                def _(dve):
                    dve.wait_ge(s["w_in"], 16 * 9)
                    dve.wait_ge(s["c_in"], 16 * 5)
                    for k in range(2):
                        for j in range(2):
                            nc.vector.tensor_scalar(adiag[:, k, j * H:(j + 1) * H], amask[:, k, :],
                                                    acol[:, k, j:j + 1], None, ALU.mult).then_inc(s["ad"], 1)
                    dve.wait_ge(s["wt_ps"], 1)
                    nc.vector.tensor_copy(wfcT[:].rearrange("p k n -> p (k n)"), ps_t[0][:]).then_inc(s["wt_sb"], 1)
                    dve.wait_ge(s["we_ps"], 1)
                    for k in range(2):
                        nc.vector.tensor_copy(wfe[:, k, 0:D], wfc[:, k, :]).then_inc(s["we_sb"], 1)
                        nc.vector.tensor_copy(wfe[:, k, D:D + 2 * H],
                                              ps_f[0][:, 16 * k:16 * k + 16]).then_inc(s["we_sb"], 1)
                    dve.sem_inc(s["x_free"], 2)

                    def pair(i, first):
                        links = [0]

                        def link(ins):
                            links[0] += 1
                            ins.then_inc(s["rs"], 1)
                            dve.wait_ge(s["rs"], i * C_RS + links[0])

                        for k in range(2):
                            t = i * 2 + k
                            dve.wait_ge(x_in[k], i * 16 + 16)
                            nc.vector.bn_stats(stat[:, k, :], xin[:, k, :]).then_inc(s["stats"], 1)
                            tick_wait(dve, s["stats"], t + 1, s["fin_v"])
                            nc.vector.bn_aggr(mv[:, k, :], stat[:, k, :]).then_inc(s["mean"], 1)
                        dve.wait_ge(s["mean"], i * 2 + 2)
                        inverse_sqrt(nc, link, mv[:, :, 1], rstd)
                        assert links[0] == C_RS
                        for k in range(2):
                            t = i * 2 + k
                            if not first:
                                tick_wait(dve, xn_st[k], i * 16, s["fin_v"])
                            nc.vector.tensor_scalar(xn[:, k, :], xin[:, k, :], mv[:, k, 0:1], rstd[:, 4, k:k + 1],
                                                    ALU.subtract, ALU.mult).then_inc(s["xn_rdy"], 1)
                            dve.wait_ge(s["xn_rdy"], t + 1)
                            dve.sem_inc(s["x_free"], 1)
                        for k in range(2):
                            t = i * 2 + k
                            dve.wait_ge(s["kv_ps"], t + 1)
                            nc.vector.tensor_tensor(kpre[:, k, :], ps_kv[k][0:P, 0:D], bkv[:, 0:D],
                                                    ALU.add).then_inc(s["k_pre"], 1)
                            nc.vector.tensor_tensor(
                                vv[:, k, :, 0:HALF], ps_kv[k][0:P, D:2 * D].rearrange("p (m c) -> p m c", m=2),
                                bkv[:, D:2 * D].rearrange("p (m c) -> p m c", m=2), ALU.add).then_inc(s["v_sb"], 1)
                            dve.wait_ge(s["k_pre"], t + 1)
                            nc.vector.tensor_scalar(kneg[:, k, :], kpre[:, k, :], 0.0, None,
                                                    ALU.min).then_inc(s["k_neg"], 1)
                        for k in range(2):
                            t = i * 2 + k
                            dve.wait_ge(s["k_exp"], t + 1)
                            nc.vector.scalar_tensor_tensor(kphi[:, k, :], kpre[:, k, :], 0.0, kexp[:, k, :],
                                                           ALU.max, ALU.add).then_inc(s["k_phi"], 1)

                    pair(0, True)
                    with dve.Fori(1, BLOCKS // 2) as i:
                        pair(i, False)
                    dve.wait_ge(s["kv_acc"], BLOCKS)
                    for m in range(2):
                        o = m * (HALF + 1)
                        nc.vector.tensor_tensor(KV[:, m, :], ps_acc[:, o:o + HALF], headmask[:],
                                                ALU.mult).then_inc(s["mgd"], 1)
                        nc.vector.tensor_scalar(KS[:, m, :], headmask[:], ps_acc[:, o + HALF:o + HALF + 1], None,
                                                ALU.mult).then_inc(s["mgd"], 1)
                    for k in range(2):
                        dve.wait_ge(xn_st[k], 16 * (BLOCKS // 2))
                    dve.wait_ge(s["f_sb"], BLOCKS)
                    nc.vector.tensor_reduce(xn[:, 0, 0:H], elr[:, 0:BLOCKS, 0:H].rearrange("p b h -> p h b"),
                                            AX.X, ALU.max).then_inc(s["mgp"], 1)
                    dve.wait_ge(s["mgt"], 1)
                    nc.vector.tensor_reduce(xn[0:H, 1, 0:1], ps_t[0][0:H, 0:P], AX.X, ALU.max).then_inc(s["mg1"], 1)
                    dve.wait_ge(s["mg1"], 1)
                    nc.vector.tensor_scalar(xn[0:H, 1, 8:16], ident[0:H, 0:H], xn[0:H, 1, 0:1], None,
                                            ALU.mult).then_inc(s["mg8"], 1)
                    dve.wait_ge(s["mgps"], 1)
                    nc.vector.tensor_copy(mg_row[:], ps_t[1][0:P, 0:H]).then_inc(s["mgd"], 1)

                @block.scalar
                def _(act):
                    def pair(i, first):
                        for k in range(2):
                            t = i * 2 + k
                            act.wait_ge(s["xt_ps"], t + 1)
                            nc.scalar.copy(xnT[:, k].rearrange("p m c -> p (m c)"),
                                           ps_t[k][:, 0:2 * P]).then_inc(s["xt_sb"], 1)
                        for k in range(2):
                            t = i * 2 + k
                            if not first:
                                tick_wait(act, f_st[k], i * 16, s["fin_a"])
                            act.wait_ge(s["f_ps"], t + 1)
                            nc.scalar.copy(fe[:, k, :], ps_f[k][0:P, 0:ROW]).then_inc(s["el_sb"], 1)
                            nc.scalar.copy(elr[:, t, :] if first else elr[:, bass.ds(t, 1), :].rearrange("p o h -> p (o h)"),
                                           ps_f[k][0:P, D:D + 2 * H]).then_inc(s["f_sb"], 1)
                        for k in range(2):
                            t = i * 2 + k
                            act.wait_ge(s["k_neg"], t + 1)
                            nc.scalar.activation(kexp[:, k, :], kneg[:, k, :], ACT.Exp).then_inc(s["k_exp"], 1)

                    pair(0, True)
                    with act.Fori(1, BLOCKS // 2) as i:
                        pair(i, False)

                @block.tensor
                def _(pe):
                    pe.wait_ge(s["w_in"], 16 * 9)
                    pe.wait_ge(s["c_in"], 16 * 5)
                    for k in range(2):
                        for m in range(2):
                            last = nc.tensor.transpose(ps_t[0][:, m * D + k * HALF:m * D + (k + 1) * HALF],
                                                       wfc[:, k, m * HALF:(m + 1) * HALF], ident[:])
                    last.then_inc(s["wt_ps"], 1)
                    pe.wait_ge(s["wt_sb"], 1)
                    pe.wait_ge(s["ad"], 4)
                    for k in range(2):
                        for m in range(2):
                            last = nc.tensor.matmul(ps_f[0][:, 16 * k:16 * k + 16],
                                                    wfcT[:, m, k * HALF:(k + 1) * HALF], adiag[:, m, :],
                                                    start=(m == 0), stop=(m == 1))
                    last.then_inc(s["we_ps"], 1)
                    pe.wait_ge(s["we_sb"], 4)
                    pe.wait_ge(s["setup"], 5)
                    nc.tensor.matmul(ps_acc[:, 0:2 * (HALF + 1)], zero[:, 0:128], zero[:], start=True, stop=False,
                                     skip_group_check=True)
                    with pe.Fori(0, BLOCKS // 2) as i:
                        for k in range(2):
                            t = i * 2 + k
                            pe.wait_ge(s["xn_rdy"], t + 1)
                            for m in range(2):
                                last = nc.tensor.transpose(ps_t[k][:, m * P:(m + 1) * P],
                                                           xn[:, k, m * HALF:(m + 1) * HALF], ident[0:P, 0:P])
                            last.then_inc(s["xt_ps"], 1)
                        for k in range(2):
                            t = i * 2 + k
                            pe.wait_ge(s["xt_sb"], t + 1)
                            for m in range(2):
                                last = nc.tensor.matmul(ps_f[k][0:P, 0:D + 2 * H], xnT[:, k, m, :], wfe[:, m, :],
                                                        start=(m == 0), stop=(m == 1))
                            last.then_inc(s["f_ps"], 1)
                            for m in range(2):
                                last = nc.tensor.matmul(ps_kv[k][0:P, :], xnT[:, k, m, :], wkv[:, m, :],
                                                        start=(m == 0), stop=(m == 1))
                            last.then_inc(s["kv_ps"], 1)
                        for k in range(2):
                            t = i * 2 + k
                            tick_wait(pe, s["v_sb"], t + 1, s["fin_p"])
                            pe.wait_ge(s["k_phi"], t + 1)
                            for m in range(2):
                                o = m * (HALF + 1)
                                last = nc.tensor.matmul(ps_acc[:, o:o + HALF + 1],
                                                        kphi[:, k, m * HALF:(m + 1) * HALF], vv[:, k, m, :],
                                                        start=False, stop=False, skip_group_check=True)
                            last.then_inc(s["kv_acc"], 1)
                    pe.wait_ge(s["mgp"], 1)
                    nc.tensor.transpose(ps_t[0][0:H, 0:P], xn[:, 0, 0:H], ident[0:P, 0:P]).then_inc(s["mgt"], 1)
                    pe.wait_ge(s["mg8"], 1)
                    nc.tensor.matmul(ps_t[1][0:P, 0:H], ones[0:H, 0:P], xn[0:H, 1, 8:16], start=True,
                                     stop=True).then_inc(s["mgps"], 1)

        with ExitStack() as st:
            dlast = sb("dlast", [100, 17], i32, where=st)
            ctile = sb("ctile", [100, 17], where=st)
            cunit = sb("cunit", [UP, UG], where=st)
            kf = sb("kf", [100, 4, 17], where=st)
            keys = sb("keys", [UP, TILES], where=st)
            less = sb("less", [UP, TILES], where=st)
            tu = sb("tu", [UP, UG], where=st)
            bu = sb("bu", [UP, UG], where=st)
            off = sb("off", [UP, UG], where=st)
            tui = sb("tui", [UP, UG], i32, where=st)
            brow = sb("brow", [1, UNITS], where=st)
            lrow = sb("lrow", [1, UNITS], where=st)
            gi = sb("gi", [UP, 4, P], i32, where=st)
            gf = sb("gf", [UP, 4, P], where=st)
            pt = [pb(f"pt{i}", st) for i in range(4)]
            s = sems(st, "b_in b_chain key_st key_ld tu_rdy tui_rdy bst bld g_in gcast gt gt_out dl_st bfin")
            with nc.Block() as block:
                @block.sync
                def _(sp):
                    with nc.allow_non_contiguous_dma(reason="one element of each tile"):
                        sp.dma_start(dlast[:].rearrange("p (c o) -> p c o", o=1),
                                     dst_tiles.rearrange("(p c) e -> p c e", c=17)[:, :, P - 1:P]).then_inc(s["b_in"], 16)
                    sp.dma_start(ctile[:], a["c_tile"]).then_inc(s["b_in"], 16)
                    sp.dma_start(cunit[:], a["c_unit"]).then_inc(s["b_in"], 16)
                    sp.wait_ge(s["b_chain"], 5)
                    sp.dma_start(key_dram.rearrange("(p c) -> p c", c=17), kf[:, 3, :]).then_inc(s["key_st"], 16)
                    sp.wait_ge(s["key_st"], 16)
                    sp.dma_start(keys[:], row(key_dram, UP)).then_inc(s["key_ld"], 16)
                    sp.wait_ge(s["tui_rdy"], 2)
                    with nc.allow_non_contiguous_dma(reason="the units' blocks, unit by unit"):
                        sp.dma_start(blk_dram.rearrange("(g p o) -> p g o", p=UP, o=1),
                                     bu[:].rearrange("p (g o) -> p g o", o=1)).then_inc(s["bst"], 16)
                    sp.wait_ge(s["bst"], 16)
                    sp.dma_start(brow[:], row(blk_dram, 1)).then_inc(s["bld"], 16)
                    for g in range(UG):
                        sp.wait_ge(s["gcast"], 2 * g + 2)
                        sp.dma_start(dl_dram[g * UP:(g + 1) * UP, :], gf[:, 2 + g % 2, :]).then_inc(s["dl_st"], 16)
                        sp.wait_ge(s["dl_st"], 16 * g + 16)

                @block.vector
                def _(dve):
                    dve.wait_ge(s["b_in"], 48)
                    nc.vector.tensor_copy(kf[:, 0, :], dlast[:]).then_inc(s["b_chain"], 1)
                    dve.wait_ge(s["b_chain"], 1)
                    nc.vector.tensor_scalar(kf[:, 1, :], kf[:, 0, :], -float(P // 2), 1.0 / P, ALU.add,
                                            ALU.mult).then_inc(s["b_chain"], 1)
                    dve.wait_ge(s["b_chain"], 2)
                    nc.vector.tensor_scalar(kf[:, 2, :], kf[:, 1, :], 12582912.0, None, ALU.add).then_inc(s["b_chain"], 1)
                    dve.wait_ge(s["b_chain"], 3)
                    nc.vector.tensor_scalar(kf[:, 1, :], kf[:, 2, :], -12582912.0, None, ALU.add).then_inc(s["b_chain"], 1)
                    dve.wait_ge(s["b_chain"], 4)
                    nc.vector.tensor_tensor(kf[:, 3, :], kf[:, 1, :], ctile[:], ALU.add).then_inc(s["b_chain"], 1)
                    dve.wait_ge(s["key_ld"], 16)
                    for g in range(UG):
                        if g:
                            dve.wait_ge(s["tu_rdy"], g)
                        nc.vector.tensor_scalar(less[:, 0:TILES - 1], keys[:, 0:TILES - 1], cunit[:, g:g + 1], 0.0,
                                                ALU.is_lt, ALU.add, accum_out=tu[:, g:g + 1]).then_inc(s["tu_rdy"], 1)
                    dve.wait_ge(s["tu_rdy"], UG)
                    nc.vector.tensor_copy(tui[:], tu[:]).then_inc(s["tui_rdy"], 1)
                    nc.vector.tensor_tensor(bu[:], cunit[:], tu[:], ALU.subtract).then_inc(s["tui_rdy"], 1)
                    dve.wait_ge(s["tui_rdy"], 2)
                    nc.vector.tensor_scalar(off[:], bu[:], float(P), None, ALU.mult).then_inc(s["b_chain"], 1)
                    dve.wait_ge(s["bld"], 16)
                    nc.vector.memset(lrow[:, UNITS - 1:UNITS], 0.0).then_inc(s["b_chain"], 1)
                    nc.vector.tensor_tensor(lrow[:, 0:UNITS - 1], brow[:, 1:UNITS], brow[:, 0:UNITS - 1],
                                            ALU.not_equal).then_inc(s["b_chain"], 1)
                    dve.wait_ge(s["b_chain"], 8)
                    nc.vector.tensor_copy(last_tab[:], lrow[:]).then_inc(s["bfin"], 1)
                    nc.vector.tensor_copy(blk_tab[:, 0:UNITS], brow[:]).then_inc(s["bfin"], 1)
                    for g in range(UG):
                        k = g % 2
                        dve.wait_ge(s["g_in"], 32 * (g + 1))
                        if g >= 2:
                            dve.wait_ge(s["gt"], 2 * (g - 1))
                            dve.wait_ge(s["dl_st"], 16 * (g - 1))
                        nc.vector.tensor_copy(gf[:, k, :], gi[:, k, :]).then_inc(s["gcast"], 1)
                        nc.vector.tensor_scalar(gf[:, 2 + k, :], gi[:, 2 + k, :], off[:, g:g + 1], None,
                                                ALU.subtract).then_inc(s["gcast"], 1)
                        dve.wait_ge(s["gt"], 2 * (g + 1))
                        nc.vector.tensor_copy(srcT[:, g * UP:(g + 1) * UP], pt[k][0:P, 0:UP]).then_inc(s["gt_out"], 1)
                        nc.vector.tensor_copy(dlT[:, g * UP:(g + 1) * UP], pt[2 + k][0:P, 0:UP]).then_inc(s["gt_out"], 1)

                @block.gpsimd
                def _(pool):
                    pool.wait_ge(s["tui_rdy"], 1)
                    for g in range(UG):
                        k = g % 2
                        if g >= 2:
                            pool.wait_ge(s["gcast"], 2 * (g - 1))
                        idx = bass.IndirectOffsetOnAxis(ap=tui[:, g:g + 1], axis=0)
                        pool.indirect_dma_start(gi[:, k, :], None, src_tiles, idx).then_inc(s["g_in"], 16)
                        pool.indirect_dma_start(gi[:, 2 + k, :], None, dst_tiles, idx).then_inc(s["g_in"], 16)
                        pool.wait_ge(s["g_in"], 32 * (g + 1))

                @block.tensor
                def _(pe):
                    for g in range(UG):
                        k = g % 2
                        pe.wait_ge(s["gcast"], 2 * (g + 1))
                        if g >= 2:
                            pe.wait_ge(s["gt_out"], 2 * (g - 1))
                        nc.tensor.transpose(pt[k][0:P, 0:UP], gf[:, k, :], ident[0:UP, 0:UP]).then_inc(s["gt"], 1)
                        nc.tensor.transpose(pt[2 + k][0:P, 0:UP], gf[:, 2 + k, :], ident[0:UP, 0:UP]).then_inc(s["gt"], 1)

        main_stage(nc, a, dict(
            sb=sb, pb=pb, sems=sems, ident=ident, halves=halves, column=column, row=row, tick_wait=tick_wait,
            xn_dram=xn_dram, dl_dram=dl_dram, table=table, out=a["out"], iota=iota, jcol=jcol, elr=elr, KV=KV, KS=KS,
            srcT=srcT, dlT=dlT, blk_tab=blk_tab, last_tab=last_tab, mg_row=mg_row))


def main_stage(nc, a, g):
    f32, i32, u32 = mybir.dt.float32, mybir.dt.int32, mybir.dt.uint32
    ALU, ACT, AX = mybir.AluOpType, mybir.ActivationFunctionType, mybir.AxisListType
    sb, ident, halves, column, row, tick_wait = g["sb"], g["ident"], g["halves"], g["column"], g["row"], g["tick_wait"]
    F2 = 2 * P
    with ExitStack() as st:
        def t_(name, shape, dt=f32):
            return sb(name, shape, dt, where=st)

        wq, wo = t_("wq", [128, 2, D]), t_("wo", [128, 2, D])
        w1, w2 = t_("w1", [128, 2, FF]), t_("w2", [128, 8, D])
        rw1, rw2 = t_("rw1", [128, 2, RH]), t_("rw2", [128, EXPERTS])
        ew = [t_(f"ew{j}", [128, EXPERTS, 2, D]) for j in range(3)]
        eb = [t_(f"eb{j}", [128, EXPERTS, 2]) for j in range(2)]
        eb3 = t_("eb3", [EXPERTS, D])
        bq, b1, rb1 = t_("bq", [128, 2]), t_("b1c", [128, 8]), t_("rb1", [128, 1])
        rows = t_("rows", [P, 7, D])
        rb2 = t_("rb2", [P, EXPERTS])
        BO, G1, B1, B2, G2, BB2, GB = range(7)
        G = t_("G", [P, RING * BATCH, ROW])
        ix = t_("ix", [P, RING * BATCH], i32)
        dlrow = t_("dlrow", [P, RING, BATCH * P])
        Sel = t_("Sel", [P, 2, P])
        ST8 = t_("ST8", [P, BATCH, P])
        sc = t_("sc", [P, 5, BATCH, H])
        xb, x2, xm = t_("xb", [P, D]), t_("x2", [P, D]), t_("xm", [P, D])
        rden, r, rneg, rexp, gpos = t_("rden", [P, 2, H]), t_("r", [P, D]), t_("rneg", [P, D]), t_("rexp", [P, D]), t_("gpos", [P, D])
        est, emv, ers = t_("est", [P, 6]), t_("emv", [P, 2]), t_("ers", [P, 5, 1])
        xmT, rhT = t_("xmT", [128, F2]), t_("rhT", [128, P])
        lg, pr, top, topi, gate = t_("lg", [P, 8]), t_("pr", [P, 8]), t_("top", [P, 8]), t_("topi", [P, 8], u32), t_("gate", [P, 8])
        rs_ = t_("rs_", [P, 12])
        lg2, gate2, zrow = t_("lg2", [P, EXPERTS]), t_("gate2", [P, 16]), t_("zrow", [128, ROW])
        gT = t_("gT", [EXPERTS, P])
        h1, h2 = t_("h1", [128, 2, 2, P]), t_("h2", [128, 2, 2, P])
        comb = t_("comb", [P, D])
        xnb, xnT = t_("xnb", [P, D]), t_("xnTm", [128, F2])
        qneg, qpos, qe, qphi = t_("qneg", [128, F2]), t_("qpos", [128, F2]), t_("qe", [128, F2]), t_("qphi", [128, F2])
        dinv, dinv2, attn = t_("dinv", [128, F2]), t_("dinv2", [128, F2]), t_("attn", [128, F2])
        t1, t2, t3, x1 = t_("t1", [P, D]), t_("t2", [P, D]), t_("t3", [P, D]), t_("x1", [P, D])
        mst, mmv, mrs = t_("mst", [P, 6]), t_("mmv", [P, 2]), t_("mrs", [P, 5, 1])
        x1T, hT = t_("x1T", [128, F2]), t_("hT", [128, 8, P])
        mixo = t_("mixo", [P, D])
        p_acc, p_er, p_a, p_b, p_h0, p_h1, p_e1, p_e2 = [g["pb"](f"pc{i}", st) for i in range(8)]
        s = g["sems"](st, "w_in dl_in dl_free ix_rdy g_in0 g_in1 g_in2 g_rdy agg er_ps st8 sel zc ee scaled er_free s_chain e_rdy comb_free r_chain "
                       "xb_in xb_free xn_in xn_free out_st out_rdy acc_free g_neg g_exp g_chain xm_rdy "
                       "m_t m_xnt m_q m_qneg m_qe m_qphi m_kv m_attn m_y m_x1 m_t2 m_x1t m_h0 m_h1 m_r0 m_r1 m_y2 "
                       "m_chain m_out e_t e_xmt e_rh e_rht e_lg r_lg r_exp r_top r_exp2 gate_rdy e_gt e_gts e_bias "
                       "h1_ps h1_sb h2_ps h2_sb o_ps o_sb tick_a tick_v tick_p tick_g tick_e zrow")
        g_in = [s["g_in0"], s["g_in1"], s["g_in2"]]
        RB = RING * BATCH
        NW = 36
        C_MIX, C_GNN, C_ROUTE = 14 + 2 * (C_RS - 1), 11 + C_RS - 1, 12

        def snap(eng, v, low, high):
            return eng.snap(v, min_val=low, max_val=high)

        def batches(eng, score, unit, block_end, before_units=None, unroll=1):
            score(0, 0)
            with eng.Fori(0, BATCHES // RING) as a_:
                with eng.Fori(0, RING) as r_:
                    n = snap(eng, a_ * RING + r_, 0, BATCHES - 1)
                    with eng.If(n < BATCHES - 1):
                        nxt = snap(eng, a_ * RING + r_ + 1, 1, BATCHES - 1)
                        score(nxt, snap(eng, (r_ + 1) % RING, 0, RING - 1))
                    if before_units:
                        before_units(n)
                    with eng.Fori(0, BATCH // unroll) as j:
                        for k in range(unroll):
                            u = snap(eng, (a_ * RING + r_) * BATCH + j * unroll + k, 0, UNITS - 1)
                            last = eng.value_load(g["last_tab"][0:1, bass.ds(u, 1)], min_val=0, max_val=1)
                            if unit:
                                unit(u, snap(eng, r_ * BATCH + j * unroll + k, 0, RB - 1), k)
                            with eng.If(last == 1):
                                b = eng.value_load(g["blk_tab"][0:1, bass.ds(u, 1)], min_val=0, max_val=BLOCKS - 1)
                                block_end(b, u)

        with nc.Block() as block:
            @block.sync
            def _(sp):
                loads = [(wq[:], halves(a["L0_mix_Wq"])), (wo[:], halves(a["L0_mix_Wo"])),
                         (w1[:], halves(a["L0_mix_W1"])), (w2[:], halves(a["L0_mix_W2"])),
                         (rw1[:], halves(a["L0_ffn_router_w1"])), (rw2[:], a["L0_ffn_router_w2"]),
                         (eb3[:], a["L0_ffn_expert_b3"]), (rb2[:], row(a["L0_ffn_router_b2"], P))]
                for j in range(3):
                    for k in range(2):
                        loads.append((ew[j][:, :, k, :],
                                      a[f"L0_ffn_expert_w{j + 1}"].rearrange("e (k p) n -> k p e n", k=2)[k]))
                for j, name in enumerate(("mix_bo", "mix_ln1_g", "mix_ln1_b", "mix_b2", "mix_ln2_g", "mix_ln2_b", "gnn_bias")):
                    loads.append((rows[:, j, :], row(a["L0_" + name], P)))
                cols = [(b1[:], column(a["L0_mix_b1"], 128)), (bq[:], column(a["L0_mix_bq"], 128)),
                        (rb1[:], column(a["L0_ffn_router_b1"], 128))]
                for j in range(2):
                    for e in range(EXPERTS):
                        cols.append((eb[j][:, e, :], column(a[f"L0_ffn_expert_b{j + 1}"][e], 128)))
                assert len(loads) + len(cols) == NW
                for dst, src in loads:
                    sp.dma_start(dst, src).then_inc(s["w_in"], 16)
                with nc.allow_non_contiguous_dma(reason="biases as columns, once"):
                    for dst, src in cols:
                        sp.dma_start(dst, src).then_inc(s["w_in"], 16)
                sp.dma_start(xnb[:], g["xn_dram"][0:P, :]).then_inc(s["xn_in"], 16)
                sp.wait_ge(s["xn_free"], 1)
                sp.dma_start(xnb[:], g["xn_dram"][P:2 * P, :]).then_inc(s["xn_in"], 16)
                sp.sem_inc(s["xb_free"], 1)
                sp.sem_inc(s["comb_free"], 1)

                def load_dl(n, slot):
                    if not isinstance(n, int):
                        tick_wait(sp, s["dl_in"], n * 16, s["tick_g"])
                        sp.wait_ge(s["dl_free"], n)
                    sp.dma_start(dlrow[:, bass.ds(slot, 1), :].rearrange("p o e -> p (o e)"),
                                 g["dl_dram"][bass.ds(n * BATCH, BATCH), :].rearrange("(o u) e -> o (u e)", o=1)
                                 .broadcast_to((P, BATCH * P))).then_inc(s["dl_in"], 16)

                def block_end(b, u):
                    sp.wait_ge(s["xb_free"], b + 1)
                    sp.dma_start(xb[:], a["x"][bass.ds(b * P, P), :]).then_inc(s["xb_in"], 16)
                    sp.wait_ge(s["xn_free"], b + 2)
                    sp.dma_start(xnb[:], g["xn_dram"][bass.ds(b * P + 2 * P, P), :]).then_inc(s["xn_in"], 16)
                    sp.wait_ge(s["out_rdy"], b + 1)
                    sp.dma_start(g["out"][bass.ds(b * P, P), :], comb[:]).then_inc(s["out_st"], 16)
                    sp.wait_ge(s["out_st"], b * 16 + 16)
                    sp.sem_inc(s["comb_free"], 1)

                batches(sp, load_dl, None, block_end)
                sp.wait_ge(s["out_st"], 16 * BLOCKS)
                sp.wait_ge(s["xn_in"], 16 * (BLOCKS + 2))

            @block.gpsimd
            def _(pool):
                def ring_turn(a_, first):
                    for k in range(RING):
                        n = a_ * RING + k
                        tick_wait(pool, s["agg"], n * BATCH + BATCH, s["tick_p"])
                        nc.gpsimd.tensor_copy(ix[:, k * BATCH:(k + 1) * BATCH],
                                              g["srcT"][:, n * BATCH:(n + 1) * BATCH] if first else
                                              g["srcT"][:, bass.ds(n * BATCH, BATCH)]).then_inc(s["ix_rdy"], 1)
                        tick_wait(pool, s["ix_rdy"], n + 1, s["tick_p"])
                        for j in range(k * BATCH, (k + 1) * BATCH):
                            pool.indirect_dma_start(G[:, j, :], None, g["table"][:, :],
                                                    bass.IndirectOffsetOnAxis(ap=ix[:, j:j + 1], axis=0)).then_inc(g_in[k], 16)
                        if k or not first:
                            before, turns = (g_in[k - 1], a_ + 1) if k else (g_in[RING - 1], a_)
                            pool.wait_ge(before, turns * (16 * BATCH))
                            pool.sem_inc(s["g_rdy"], 1)

                ring_turn(0, True)
                with pool.Fori(1, BATCHES // RING) as a_:
                    ring_turn(a_, False)
                pool.wait_ge(g_in[RING - 1], (BATCHES // RING) * 16 * BATCH)
                pool.sem_inc(s["g_rdy"], 1)

            @block.vector
            def _(dve):
                TT, TS, STT, CP = (nc.vector.tensor_tensor, nc.vector.tensor_scalar,
                                   nc.vector.scalar_tensor_tensor, nc.vector.tensor_copy)

                def chained(sem, base):
                    count = [0]

                    def link(ins):
                        count[0] += 1
                        ins.then_inc(sem, 1)
                        dve.wait_ge(sem, base + count[0])
                    return link, count

                nc.vector.memset(zrow[:], 0.0).then_inc(s["zrow"], 1)
                dve.wait_ge(s["w_in"], 16 * NW)

                def score(n, slot):
                    n1 = n + 1
                    Gs = G[:, bass.ds(slot * BATCH, BATCH), :]
                    tick_wait(dve, s["er_ps"], n + 1, s["tick_v"])
                    dve.wait_ge(s["dl_in"], n * 16 + 16)
                    TS(ST8[:].rearrange("p u c -> p (u c)"),
                       dlrow[:, bass.ds(slot, 1), :].rearrange("p o e -> p (o e)"), g["jcol"][:, 0:1], None,
                       ALU.is_equal).then_inc(s["st8"], 1)
                    dve.wait_ge(s["st8"], n1)
                    dve.sem_inc(s["dl_free"], 1)
                    tick_wait(dve, s["er_ps"], n + 2, s["tick_v"])
                    er = p_er[0:P, 0:BATCH * H].rearrange("p (u h) -> p u h", h=H)
                    dve.wait_ge(s["g_rdy"], n1)
                    TT(sc[:, 0], er, Gs[:, :, D:ROW], ALU.add).then_inc(s["er_free"], 1)
                    TT(sc[:, 1], er, g["mg_row"][:].rearrange("p (o h) -> p o h", o=1).broadcast_to((P, BATCH, H)),
                       ALU.add).then_inc(s["er_free"], 1)
                    dve.wait_ge(s["er_free"], n * 2 + 4)
                    STT(sc[:, 2], sc[:, 0], SLOPE, sc[:, 0], ALU.mult, ALU.max).then_inc(s["s_chain"], 1)
                    STT(sc[:, 3], sc[:, 1], SLOPE, sc[:, 1], ALU.mult, ALU.max).then_inc(s["s_chain"], 1)
                    dve.wait_ge(s["s_chain"], n * 2 + 2)
                    TT(sc[:, 4], sc[:, 2], sc[:, 3], ALU.subtract).then_inc(s["e_rdy"], 1)
                    dve.wait_ge(s["ee"], n1)
                    ee = Gs[:, :, D:ROW].rearrange("p u (h o) -> p u h o", o=1).broadcast_to((P, BATCH, H, DH))
                    Gv = Gs[:, :, 0:D].rearrange("p u (h c) -> p u h c", h=H)
                    TT(Gv, Gv, ee, ALU.mult).then_inc(s["scaled"], 1)

                def norm_stats(link, src, stats, mean, rs):
                    link(nc.vector.bn_stats(stats[:], src))
                    dve.sem_inc(s["tick_v"], 1)
                    link(nc.vector.bn_aggr(mean[:], stats[:]))
                    inverse_sqrt(nc, link, mean[:, 1:2], rs)

                def mix_q(n1):
                    dve.wait_ge(s["m_q"], n1)
                    for m in range(2):
                        TS(qneg[:, m * P:(m + 1) * P], p_b[:, m * P:(m + 1) * P], bq[:, m:m + 1], 0.0, ALU.add,
                           ALU.min).then_inc(s["m_qneg"], 1)
                        TS(qpos[:, m * P:(m + 1) * P], p_b[:, m * P:(m + 1) * P], bq[:, m:m + 1], 0.0, ALU.add,
                           ALU.max).then_inc(s["m_qneg"], 1)

                def mix_phi(n1):
                    dve.wait_ge(s["m_qneg"], n1 * 4)
                    dve.sem_inc(s["tick_v"], 1)
                    dve.wait_ge(s["m_qe"], n1)
                    TT(qphi[:], qe[:], qpos[:], ALU.add).then_inc(s["m_qphi"], 1)

                def mix_attn(n1, link):
                    dve.wait_ge(s["m_kv"], n1)
                    link(TS(dinv[:], p_a[:, F2:2 * F2], ATT_EPS, None, ALU.add))
                    link(nc.vector.reciprocal(dinv2[:], dinv[:]))
                    TT(attn[:], p_a[:, 0:F2], dinv2[:], ALU.mult).then_inc(s["m_attn"], 1)

                def mix_norm1(n1, link):
                    dve.wait_ge(s["m_y"], n1)
                    link(TT(t1[:], p_b[0:P, 0:D], xnb[:], ALU.add))
                    dve.sem_inc(s["xn_free"], 1)
                    link(TT(t2[:], t1[:], rows[:, BO, :], ALU.add))
                    norm_stats(link, t2[:], mst, mmv, mrs)
                    link(STT(t3[:], t2[:], mmv[:, 0:1], rows[:, G1, :], ALU.subtract, ALU.mult))
                    STT(x1[:], t3[:], mrs[:, 4, :], rows[:, B1, :], ALU.mult, ALU.add).then_inc(s["m_x1"], 1)

                def mix_relu(n1):
                    dve.wait_ge(s["m_h1"], n1)
                    for m in range(4, 8):
                        last = TS(hT[:, m, :], p_h1[:, (m - 4) * P:(m - 3) * P], b1[:, m:m + 1], 0.0, ALU.add, ALU.max)
                    last.then_inc(s["m_r1"], 1)

                def mix_norm2(n1, link):
                    dve.wait_ge(s["m_x1"], n1)
                    dve.sem_inc(s["tick_v"], 1)
                    dve.wait_ge(s["m_y2"], n1)
                    link(TT(t1[:], p_b[0:P, 0:D], x1[:], ALU.add))
                    link(TT(t2[:], t1[:], rows[:, B2, :], ALU.add))
                    norm_stats(link, t2[:], mst, mmv, mrs)
                    link(STT(t3[:], t2[:], mmv[:, 0:1], rows[:, G2, :], ALU.subtract, ALU.mult))
                    STT(mixo[:], t3[:], mrs[:, 4, :], rows[:, BB2, :], ALU.mult, ALU.add).then_inc(s["m_out"], 1)

                def graph_end(b, u, link):
                    dve.wait_ge(s["agg"], u + (RB + 1))
                    link(TS(rden[:, 0, :], p_acc[0:P, D:ROW], TINY, None, ALU.max))
                    link(nc.vector.reciprocal(rden[:, 1, :], rden[:, 0, :]))
                    link(TT(r[:].rearrange("p (h c) -> p h c", h=H),
                            p_acc[0:P, 0:D].rearrange("p (h c) -> p h c", h=H),
                            rden[:, 1, :].rearrange("p (h o) -> p h o", o=1).broadcast_to((P, H, DH)), ALU.mult))
                    dve.sem_inc(s["acc_free"], 1)
                    link(TT(gpos[:], r[:], rows[:, GB, :], ALU.add))
                    TS(rneg[:], gpos[:], 0.0, None, ALU.min).then_inc(s["g_neg"], 1)

                def graph_out(b, link):
                    dve.wait_ge(s["g_exp"], b + 1)
                    link(TS(r[:], gpos[:], 0.0, -1.0, ALU.max, ALU.add))
                    link(TT(gpos[:], r[:], rexp[:], ALU.add))
                    dve.sem_inc(s["tick_v"], 1)
                    dve.wait_ge(s["xb_in"], b * 16 + 16)
                    link(TT(r[:], gpos[:], xb[:], ALU.add))
                    dve.sem_inc(s["xb_free"], 1)
                    dve.wait_ge(s["m_out"], b + 1)
                    link(TT(x2[:], r[:], mixo[:], ALU.add))
                    norm_stats(link, x2[:], est, emv, ers)
                    TS(xm[:], x2[:], emv[:, 0:1], ers[:, 4, :], ALU.subtract, ALU.mult).then_inc(s["xm_rdy"], 1)

                def router(b, link):
                    dve.wait_ge(s["e_lg"], b + 1)
                    link(TT(lg[:, 0:EXPERTS], p_er[0:P, F2:F2 + EXPERTS], rb2[:], ALU.add))
                    link(nc.vector.tensor_reduce(rs_[:, 10:11], lg[:, 0:EXPERTS], AX.X, ALU.max))
                    TS(rs_[:, 0:1], rs_[:, 10:11], -1.0, None, ALU.mult).then_inc(s["r_lg"], 1)
                    dve.wait_ge(s["r_exp"], b + 1)
                    link(nc.vector.reciprocal(rs_[:, 2:3], rs_[:, 1:2]))
                    link(TS(pr[:, 0:EXPERTS], lg2[:], rs_[:, 2:3], None, ALU.mult))
                    dve.sem_inc(s["tick_v"], 1)
                    link(nc.vector.max(top[:], pr[:]))
                    TT(rs_[:, 3:4], top[:, 1:2], top[:, 0:1], ALU.subtract).then_inc(s["r_top"], 1)
                    link(nc.vector.max_index(topi[:], top[:], pr[:]))
                    dve.wait_ge(s["r_exp2"], b + 1)
                    link(TS(rs_[:, 5:6], rs_[:, 4:5], 1.0, None, ALU.add))
                    link(nc.vector.reciprocal(rs_[:, 6:7], rs_[:, 5:6]))
                    link(TT(rs_[:, 7:8], rs_[:, 6:7], rs_[:, 4:5], ALU.mult))
                    link(CP(rs_[:, 8:10], topi[:, 0:2]))
                    link(TS(gate2[:, 0:EXPERTS], g["iota"][:, 0:EXPERTS], rs_[:, 8:9], rs_[:, 6:7], ALU.is_equal, ALU.mult))
                    link(TS(gate2[:, 8:8 + EXPERTS], g["iota"][:, 0:EXPERTS], rs_[:, 9:10], rs_[:, 7:8], ALU.is_equal, ALU.mult))
                    TT(gate[:, 0:EXPERTS], gate2[:, 0:EXPERTS], gate2[:, 8:8 + EXPERTS], ALU.add).then_inc(s["gate_rdy"], 1)

                def hidden2(b, e):
                    dve.wait_ge(s["h2_ps"], b * EXPERTS + (e + 1))
                    for m in range(2):
                        last = TS(h2[:, e % 2, m, :], p_e2[:, m * P:(m + 1) * P], eb[1][:, e, m:m + 1], 0.0,
                                  ALU.add, ALU.max)
                    last.then_inc(s["h2_sb"], 1)

                def base(b):
                    dve.wait_ge(s["e_bias"], b + 1)
                    dve.sem_inc(s["tick_v"], 1)
                    dve.wait_ge(s["comb_free"], b + 1)
                    TT(comb[:], x2[:], p_er[0:P, D:2 * D], ALU.add).then_inc(s["o_sb"], 1)

                def add_expert(b, e):
                    dve.wait_ge(s["o_sb"], b * (EXPERTS + 1) + (e + 1))
                    dve.sem_inc(s["tick_v"], 1)
                    dve.wait_ge(s["o_ps"], b * EXPERTS + (e + 1))
                    STT(comb[:], p_er[0:P, D:2 * D], gate[:, e:e + 1], comb[:], ALU.mult, ALU.add).then_inc(s["o_sb"], 1)
                    if e == EXPERTS - 1:
                        dve.wait_ge(s["o_sb"], b * (EXPERTS + 1) + (EXPERTS + 1))
                        dve.sem_inc(s["out_rdy"], 1)

                def block_end(b, u):
                    n1 = snap(dve, b + 2, 2, BLOCKS + 1)
                    glink, gc = chained(s["g_chain"], b * C_GNN)
                    rlink, rc = chained(s["r_chain"], b * C_ROUTE)
                    mlink, mc = chained(s["m_chain"], b * C_MIX + C_MIX)
                    graph_end(b, u, glink)
                    mix_q(n1)
                    graph_out(b, glink)
                    mix_phi(n1)
                    mix_attn(n1, mlink)
                    router(b, rlink)
                    mix_norm1(n1, mlink)
                    base(b)
                    hidden2(b, 0)
                    for e in range(2, EXPERTS + 2):
                        if e == 3:
                            mix_relu(n1)
                        if e == 5:
                            mix_norm2(n1, mlink)
                        add_expert(b, e - 2)
                        if e <= EXPERTS:
                            hidden2(b, e - 1)
                    assert (gc[0], rc[0], mc[0]) == (C_GNN, C_ROUTE, C_MIX), (gc, rc, mc)

                def unit(u, slot, k):
                    dve.wait_ge(s["agg"], u + (RB - 1))
                    TS(Sel[:, bass.ds(u % 2, 1), :].rearrange("p o c -> p (o c)"), g["iota"][:],
                       g["dlT"][:, bass.ds(u, 1)], None, ALU.is_equal).then_inc(s["sel"], 1)

                nc.vector.memset(pr[:], -1.0).then_inc(s["zrow"], 1)
                dve.wait_ge(s["zrow"], 2)
                mlink, _ = chained(s["m_chain"], 0)
                mix_q(1)
                mix_phi(1)
                mix_attn(1, mlink)
                mix_norm1(1, mlink)
                mix_relu(1)
                mix_norm2(1, mlink)
                batches(dve, score, unit, block_end)

            @block.scalar
            def _(act):
                def hidden1(b, e):
                    act.wait_ge(s["h1_ps"], b * EXPERTS + (e + 1))
                    for m in range(2):
                        last = nc.scalar.activation(h1[:, e % 2, m, :], p_e1[:, m * P:(m + 1) * P], ACT.Relu,
                                                    bias=eb[0][:, e, m:m + 1])
                    last.then_inc(s["h1_sb"], 1)

                def move(wait, n1, dst, src, done):
                    act.wait_ge(wait, n1)
                    nc.scalar.copy(dst, src).then_inc(done, 1)

                def expo(wait, n1, dst, src, done):
                    act.wait_ge(wait, n1)
                    nc.scalar.activation(dst, src, ACT.Exp).then_inc(done, 1)

                def mix_relu(n1):
                    act.wait_ge(s["m_h0"], n1)
                    for m in range(4):
                        last = nc.scalar.activation(hT[:, m, :], p_h0[:, m * P:(m + 1) * P], ACT.Relu, bias=b1[:, m:m + 1])
                    last.then_inc(s["m_r0"], 1)

                def score(n, slot):
                    act.wait_ge(s["e_rdy"], n + 1)
                    nc.scalar.activation(G[:, bass.ds(slot * BATCH, BATCH), D:ROW], sc[:, 4], ACT.Exp).then_inc(s["ee"], 1)

                def block_end(b, u):
                    n1 = snap(act, b + 2, 2, BLOCKS + 1)
                    move(s["m_t"], n1, xnT[:], p_a[:, 0:F2], s["m_xnt"])
                    expo(s["g_neg"], b + 1, rexp[:], rneg[:], s["g_exp"])
                    expo(s["m_qneg"], n1 * 4, qe[:], qneg[:], s["m_qe"])
                    move(s["e_t"], b + 1, xmT[:], p_er[:, D:D + F2], s["e_xmt"])
                    act.wait_ge(s["e_rh"], b + 1)
                    nc.scalar.activation(rhT[:], p_e2[:, D:D + P], ACT.Relu, bias=rb1[:]).then_inc(s["e_rht"], 1)
                    hidden1(b, 0)
                    act.wait_ge(s["r_lg"], b + 1)
                    nc.scalar.activation(lg2[:], lg[:, 0:EXPERTS], ACT.Exp, bias=rs_[:, 0:1],
                                         accum_out=rs_[:, 1:2]).then_inc(s["r_exp"], 1)
                    expo(s["r_top"], b + 1, rs_[:, 4:5], rs_[:, 3:4], s["r_exp2"])
                    move(s["e_gt"], b + 1, gT[:], p_er[0:EXPERTS, D:D + P], s["e_gts"])
                    hidden1(b, 1)
                    move(s["m_t2"], n1, x1T[:], p_a[:, 0:F2], s["m_x1t"])
                    for e in range(2, EXPERTS):
                        if e == 3:
                            mix_relu(n1)
                        if e < EXPERTS:
                            hidden1(b, e)

                act.wait_ge(s["w_in"], 16 * NW)
                move(s["m_t"], 1, xnT[:], p_a[:, 0:F2], s["m_xnt"])
                expo(s["m_qneg"], 4, qe[:], qneg[:], s["m_qe"])
                move(s["m_t2"], 1, x1T[:], p_a[:, 0:F2], s["m_x1t"])
                mix_relu(1)
                batches(act, score, None, block_end)

            @block.tensor
            def _(pe):
                MM, TR = nc.tensor.matmul, nc.tensor.transpose

                def two_halves(out, weights, xT, done):
                    for m in range(2):
                        for k in range(2):
                            last = MM(out[:, m * P:(m + 1) * P], weights[k][:, m * HALF:(m + 1) * HALF], xT[k],
                                      start=(k == 0), stop=(k == 1))
                    last.then_inc(done, 1)

                def parts(xT):
                    return [xT[:, 0:P], xT[:, P:F2]]

                def transposed(out, src, done):
                    for k in range(2):
                        last = TR(out[:, k * P:(k + 1) * P], src[:, k * HALF:(k + 1) * HALF], ident[0:P, 0:P])
                    last.then_inc(done, 1)

                def mix_t(n1):
                    pe.wait_ge(s["xn_in"], n1 * 16)
                    transposed(p_a, xnb, s["m_t"])

                def mix_q(n1):
                    pe.wait_ge(s["m_xnt"], n1)
                    two_halves(p_b, [wq[:, 0, :], wq[:, 1, :]], parts(xnT), s["m_q"])

                def mix_kv(n1):
                    pe.wait_ge(s["m_qphi"], n1)
                    for w, o in ((g["KV"], 0), (g["KS"], F2)):
                        for m in range(2):
                            last = MM(p_a[:, o + m * P:o + (m + 1) * P], w[:, m, :], qphi[:, m * P:(m + 1) * P],
                                      start=True, stop=True)
                    last.then_inc(s["m_kv"], 1)

                def mix_o(n1):
                    pe.wait_ge(s["m_attn"], n1)
                    for m in range(2):
                        last = MM(p_b[0:P, 0:D], attn[:, m * P:(m + 1) * P], wo[:, m, :], start=(m == 0), stop=(m == 1))
                    last.then_inc(s["m_y"], 1)

                def mix_t2(n1):
                    pe.wait_ge(s["m_x1"], n1)
                    transposed(p_a, x1, s["m_t2"])

                def mix_up(n1, lo, done):
                    pe.wait_ge(s["m_x1t"], n1)
                    p_ = p_h0 if lo == 0 else p_h1
                    for m in range(lo, lo + 4):
                        for k in range(2):
                            last = MM(p_[:, (m - lo) * P:(m - lo + 1) * P], w1[:, k, m * HALF:(m + 1) * HALF],
                                      x1T[:, k * P:(k + 1) * P], start=(k == 0), stop=(k == 1))
                    last.then_inc(done, 1)

                def mix_down(n1):
                    pe.wait_ge(s["m_r0"], n1)
                    for m in range(8):
                        if m == 4:
                            pe.wait_ge(s["m_r1"], n1)
                        last = MM(p_b[0:P, 0:D], hT[:, m, :], w2[:, m, :], start=(m == 0), stop=(m == 7))
                    last.then_inc(s["m_y2"], 1)

                def hidden1(b, e):
                    if e:
                        pe.wait_ge(s["h1_sb"], b * EXPERTS + e)
                    two_halves(p_e1, [ew[0][:, e, 0, :], ew[0][:, e, 1, :]], parts(xmT), s["h1_ps"])

                def hidden2(b, e):
                    pe.wait_ge(s["h1_sb"], b * EXPERTS + (e + 1))
                    two_halves(p_e2, [ew[1][:, e, 0, :], ew[1][:, e, 1, :]],
                               [h1[:, e % 2, 0, :], h1[:, e % 2, 1, :]], s["h2_ps"])

                def expert_out(b, e):
                    tick_wait(pe, s["h2_sb"], b * EXPERTS + (e + 1), s["tick_e"])
                    pe.wait_ge(s["o_sb"], b * (EXPERTS + 1) + (e + 1))
                    for k in range(2):
                        last = MM(p_er[0:P, D:2 * D], h2[:, e % 2, k, :], ew[2][:, e, k, :], start=(k == 0), stop=(k == 1))
                    last.then_inc(s["o_ps"], 1)

                def open_sums():
                    MM(p_acc[:, 0:ROW], zrow[:, 0:128], zrow[:], start=True, stop=False, skip_group_check=True)

                def score(n, slot):
                    blocks_of = [pe.value_load(g["blk_tab"][0:1, bass.ds(n * BATCH + j, 1)], min_val=0, max_val=BLOCKS)
                                 for j in range(BATCH)]
                    tick_wait(pe, s["er_free"], n * 2 + 2, s["tick_e"])
                    pe.wait_ge(s["st8"], n + 1)
                    for j in range(BATCH):
                        last = MM(p_er[0:P, j * H:(j + 1) * H], ST8[:, j, :],
                                  g["elr"][:, bass.ds(blocks_of[j], 1), H:2 * H].rearrange("p o h -> p (o h)"),
                                  start=True, stop=True)
                    last.then_inc(s["er_ps"], 1)

                def before_units(n):
                    pe.wait_ge(s["scaled"], n + 1)
                    pe.sem_inc(s["tick_e"], 1)

                def unit(u, slot, k):
                    pe.wait_ge(s["sel"], u + 1)
                    MM(p_acc[0:P, 0:ROW], Sel[:, k, :], G[:, bass.ds(slot, 1), :].rearrange("p o c -> p (o c)"),
                       start=False, stop=False, skip_group_check=True).then_inc(s["agg"], 1)

                def block_end(b, u):
                    n1 = snap(pe, b + 2, 2, BLOCKS + 1)
                    mix_t(n1)
                    mix_q(n1)
                    pe.wait_ge(s["xm_rdy"], b + 1)
                    transposed(p_er[:, D:], xm, s["e_t"])
                    mix_kv(n1)
                    pe.wait_ge(s["e_xmt"], b + 1)
                    for k in range(2):
                        last = MM(p_e2[:, D:D + P], rw1[:, k, :], xmT[:, k * P:(k + 1) * P], start=(k == 0), stop=(k == 1))
                    last.then_inc(s["e_rh"], 1)
                    hidden1(b, 0)
                    pe.wait_ge(s["e_rht"], b + 1)
                    MM(p_er[0:P, F2:F2 + EXPERTS], rhT[:], rw2[:], start=True, stop=True).then_inc(s["e_lg"], 1)
                    mix_o(n1)
                    hidden1(b, 1)
                    hidden2(b, 0)
                    pe.wait_ge(s["gate_rdy"], b + 1)
                    TR(p_er[0:EXPERTS, D:D + P], gate[:, 0:EXPERTS], ident[0:P, 0:P]).then_inc(s["e_gt"], 1)
                    mix_t2(n1)
                    pe.wait_ge(s["e_gts"], b + 1)
                    MM(p_er[0:P, D:2 * D], gT[:], eb3[:], start=True, stop=True).then_inc(s["e_bias"], 1)
                    mix_up(n1, 0, s["m_h0"])
                    for e in range(2, EXPERTS + 2):
                        if e == 3:
                            mix_up(n1, 4, s["m_h1"])
                        if e == 4:
                            mix_down(n1)
                        if e < EXPERTS:
                            hidden1(b, e)
                        expert_out(b, e - 2)
                        if e <= EXPERTS:
                            hidden2(b, e - 1)
                    pe.wait_ge(s["acc_free"], b + 1)
                    open_sums()

                pe.wait_ge(s["w_in"], 16 * NW)
                pe.wait_ge(s["zrow"], 2)
                open_sums()
                pe.sem_inc(s["agg"], RB)
                pe.sem_inc(s["er_ps"], 1)
                pe.sem_inc(s["er_free"], 2)
                mix_t(1)
                mix_q(1)
                mix_kv(1)
                mix_o(1)
                mix_t2(1)
                mix_up(1, 0, s["m_h0"])
                mix_up(1, 4, s["m_h1"])
                mix_down(1)
                batches(pe, score, unit, block_end, before_units, unroll=2)


def kernel(**inputs):
    import concourse.bacc as _bacc
    from concourse.bass_utils import run_bass_kernel_spmd as _run

    nc = _bacc.Bacc("TRN2", target_bir_lowering=False, num_devices=1)
    given = {k: v for k, v in inputs.items() if not k.startswith("L0_gnn_sem")}
    given.update(shape_constants())
    arrays, aps = {}, {}
    for name, value in given.items():
        v = np.ascontiguousarray(value)
        arrays["in_" + name] = v
        aps[name] = nc.dram_tensor("in_" + name, v.shape, mybir.dt.from_np(v.dtype), kind="ExternalInput").ap()
    aps["out"] = nc.dram_tensor("out_0", (N, D), mybir.dt.float32, kind="ExternalOutput").ap()
    build(nc, aps)
    r = _run(nc, [arrays], core_ids=[0])
    return r.results[0]["out_0"]
```
